# Optimizing a Trainium2 kernel written in Bass

```python
import numpy as np
import jax
import jax.numpy as jnp

def _softmax(x, axis=-1):
    return jax.nn.softmax(x, axis=axis)

def _gelu(x):
    return jax.nn.gelu(x, approximate=True)

def _silu(x):
    return jax.nn.silu(x)

def _sigmoid(x):
    return jax.nn.sigmoid(x)

def _layernorm(x, axis=-1, eps=1e-05):
    m = jnp.mean(x, axis=axis, keepdims=True)
    v = jnp.var(x, axis=axis, keepdims=True)
    return (x - m) / jnp.sqrt(v + eps)

def _scatter_add(tgt, idx, src, axis=0):
    return tgt.at[idx].add(src)

def _segment_sum(src, seg, n):
    return jax.ops.segment_sum(src, seg, n)
kernel_name = 'mk_sandwich_d1_jaxref_r4_6f7819'

def setup_inputs(seed: int=0):
    np.random.seed(seed)
    _w = jnp.asarray

    def _L0_attn_setup():
        import jax, jax.numpy as jnp
        import numpy as np
        from jax import lax
        D_MODEL = 256
        D_STATE = 16
        D_CONV = 4
        EXPAND = 2
        D_INNER = EXPAND * D_MODEL
        DT_RANK = (D_MODEL + 15) // 16
        LN_EPS = 1e-05

        def _mamba_block(x, ln_g, ln_b, W_in, conv_w, conv_b, W_xproj, W_dt, b_dt, A_log, D, W_out):
            B, L, _ = x.shape
            mu = jnp.mean(x, axis=-1, keepdims=True)
            var = jnp.var(x, axis=-1, keepdims=True)
            h = (x - mu) * lax.rsqrt(var + LN_EPS) * ln_g + ln_b
            xz = jnp.einsum('bld,de->ble', h, W_in)
            u, z = jnp.split(xz, 2, axis=-1)
            u_t = jnp.transpose(u, (0, 2, 1))
            u_t = lax.conv_general_dilated(u_t, conv_w, window_strides=(1,), padding=[(D_CONV - 1, 0)], feature_group_count=D_INNER, dimension_numbers=('NCH', 'OIH', 'NCH'))
            u_t = u_t + conv_b[None, :, None]
            u = jax.nn.silu(jnp.transpose(u_t, (0, 2, 1)))
            x_dbl = jnp.einsum('bld,de->ble', u, W_xproj)
            dt, Bm, Cm = jnp.split(x_dbl, [DT_RANK, DT_RANK + D_STATE], axis=-1)
            dt = jax.nn.softplus(jnp.einsum('blr,rd->bld', dt, W_dt) + b_dt)
            A = -jnp.exp(A_log)
            dA = jnp.exp(jnp.einsum('bld,dn->bldn', dt, A))
            dBu = jnp.einsum('bld,bln->bldn', dt * u, Bm)

            def step(hc, inp):
                dA_t, dBu_t, C_t = inp
                hc = dA_t * hc + dBu_t
                y_t = jnp.einsum('bdn,bn->bd', hc, C_t)
                return (hc, y_t)
            h0 = jnp.zeros((B, D_INNER, D_STATE), x.dtype)
            xs = (jnp.transpose(dA, (1, 0, 2, 3)), jnp.transpose(dBu, (1, 0, 2, 3)), jnp.transpose(Cm, (1, 0, 2)))
            _, ys = lax.scan(step, h0, xs)
            y = jnp.transpose(ys, (1, 0, 2)) + u * D
            y = y * jax.nn.silu(z)
            out = jnp.einsum('bld,dm->blm', y, W_out)
            return x + out
        key = jax.random.key(seed)
        ks = jax.random.split(key, 12)
        s = 0.02
        x = jax.random.normal(ks[0], (2, 512, D_MODEL), dtype=jnp.float32)
        params = {'x': x, 'ln_g': jnp.ones((D_MODEL,), jnp.float32), 'ln_b': jnp.zeros((D_MODEL,), jnp.float32), 'W_in': jax.random.normal(ks[1], (D_MODEL, 2 * D_INNER), jnp.float32) * s, 'conv_w': jax.random.normal(ks[2], (D_INNER, 1, D_CONV), jnp.float32) * 0.2, 'conv_b': jnp.zeros((D_INNER,), jnp.float32), 'W_xproj': jax.random.normal(ks[3], (D_INNER, DT_RANK + 2 * D_STATE), jnp.float32) * s, 'W_dt': jax.random.normal(ks[4], (DT_RANK, D_INNER), jnp.float32) * 0.1, 'b_dt': jax.random.normal(ks[5], (D_INNER,), jnp.float32) * 0.1, 'A_log': jnp.log(jnp.tile(jnp.arange(1.0, D_STATE + 1.0, dtype=jnp.float32), (D_INNER, 1))), 'D': jnp.ones((D_INNER,), jnp.float32), 'W_out': jax.random.normal(ks[6], (D_INNER, D_MODEL), jnp.float32) * s}
        return params
    _L0_attn_in = _L0_attn_setup()

    def _L0_ffn_setup():
        import jax, jax.numpy as jnp
        import numpy as np
        SWIGLU_ALPHA = 1.702
        SWIGLU_LIMIT = 7.0
        TOP_K = 4
        key = jax.random.key(seed)
        k = jax.random.split(key, 5)
        B, S, D, E, I = (2, 256, 256, 8, 512)
        return {'hidden_states': jax.random.normal(k[0], (B, S, D), dtype=jnp.float32), 'router_weight': jax.random.normal(k[1], (E, D), dtype=jnp.float32) * 0.02, 'router_bias': jnp.zeros((E,), dtype=jnp.float32), 'gate_up_proj': jax.random.normal(k[2], (E, 2 * I, D), dtype=jnp.float32) * 0.02, 'gate_up_proj_bias': jnp.zeros((E, 2 * I), dtype=jnp.float32), 'down_proj': jax.random.normal(k[3], (E, D, I), dtype=jnp.float32) * 0.02, 'down_proj_bias': jnp.zeros((E, D), dtype=jnp.float32)}
    _L0_ffn_in = _L0_ffn_setup()
    _d = {'L0_attn_x': _L0_attn_in['x'], 'L0_attn_ln_g': _L0_attn_in['ln_g'], 'L0_attn_ln_b': _L0_attn_in['ln_b'], 'L0_attn_W_in': _L0_attn_in['W_in'], 'L0_attn_conv_w': _L0_attn_in['conv_w'], 'L0_attn_conv_b': _L0_attn_in['conv_b'], 'L0_attn_W_xproj': _L0_attn_in['W_xproj'], 'L0_attn_W_dt': _L0_attn_in['W_dt'], 'L0_attn_b_dt': _L0_attn_in['b_dt'], 'L0_attn_A_log': _L0_attn_in['A_log'], 'L0_attn_D': _L0_attn_in['D'], 'L0_attn_W_out': _L0_attn_in['W_out'], 'L0_ffn_router_weight': _L0_ffn_in['router_weight'], 'L0_ffn_router_bias': _L0_ffn_in['router_bias'], 'L0_ffn_gate_up_proj': _L0_ffn_in['gate_up_proj'], 'L0_ffn_gate_up_proj_bias': _L0_ffn_in['gate_up_proj_bias'], 'L0_ffn_down_proj': _L0_ffn_in['down_proj'], 'L0_ffn_down_proj_bias': _L0_ffn_in['down_proj_bias']}
    _x0 = _d['L0_attn_x']
    _d['L0_attn_x'] = jax.random.normal(jax.random.fold_in(jax.random.key(seed), 1), (2, 4096, 256), dtype=_x0.dtype)
    del _x0
    return _d

def reference(L0_attn_x, L0_attn_ln_g, L0_attn_ln_b, L0_attn_W_in, L0_attn_conv_w, L0_attn_conv_b, L0_attn_W_xproj, L0_attn_W_dt, L0_attn_b_dt, L0_attn_A_log, L0_attn_D, L0_attn_W_out, L0_ffn_router_weight, L0_ffn_router_bias, L0_ffn_gate_up_proj, L0_ffn_gate_up_proj_bias, L0_ffn_down_proj, L0_ffn_down_proj_bias):

    def _L0_attn_ref(x, ln_g, ln_b, W_in, conv_w, conv_b, W_xproj, W_dt, b_dt, A_log, D, W_out):
        import jax, jax.numpy as jnp
        import numpy as np
        from jax import lax
        D_MODEL = 256
        D_STATE = 16
        D_CONV = 4
        EXPAND = 2
        D_INNER = EXPAND * D_MODEL
        DT_RANK = (D_MODEL + 15) // 16
        LN_EPS = 1e-05

        def _mamba_block(x, ln_g, ln_b, W_in, conv_w, conv_b, W_xproj, W_dt, b_dt, A_log, D, W_out):
            B, L, _ = x.shape
            mu = jnp.mean(x, axis=-1, keepdims=True)
            var = jnp.var(x, axis=-1, keepdims=True)
            h = (x - mu) * lax.rsqrt(var + LN_EPS) * ln_g + ln_b
            xz = jnp.einsum('bld,de->ble', h, W_in)
            u, z = jnp.split(xz, 2, axis=-1)
            u_t = jnp.transpose(u, (0, 2, 1))
            u_t = lax.conv_general_dilated(u_t, conv_w, window_strides=(1,), padding=[(D_CONV - 1, 0)], feature_group_count=D_INNER, dimension_numbers=('NCH', 'OIH', 'NCH'))
            u_t = u_t + conv_b[None, :, None]
            u = jax.nn.silu(jnp.transpose(u_t, (0, 2, 1)))
            x_dbl = jnp.einsum('bld,de->ble', u, W_xproj)
            dt, Bm, Cm = jnp.split(x_dbl, [DT_RANK, DT_RANK + D_STATE], axis=-1)
            dt = jax.nn.softplus(jnp.einsum('blr,rd->bld', dt, W_dt) + b_dt)
            A = -jnp.exp(A_log)
            dA = jnp.exp(jnp.einsum('bld,dn->bldn', dt, A))
            dBu = jnp.einsum('bld,bln->bldn', dt * u, Bm)

            def step(hc, inp):
                dA_t, dBu_t, C_t = inp
                hc = dA_t * hc + dBu_t
                y_t = jnp.einsum('bdn,bn->bd', hc, C_t)
                return (hc, y_t)
            h0 = jnp.zeros((B, D_INNER, D_STATE), x.dtype)
            xs = (jnp.transpose(dA, (1, 0, 2, 3)), jnp.transpose(dBu, (1, 0, 2, 3)), jnp.transpose(Cm, (1, 0, 2)))
            _, ys = lax.scan(step, h0, xs)
            y = jnp.transpose(ys, (1, 0, 2)) + u * D
            y = y * jax.nn.silu(z)
            out = jnp.einsum('bld,dm->blm', y, W_out)
            return x + out
        return _mamba_block(x, ln_g, ln_b, W_in, conv_w, conv_b, W_xproj, W_dt, b_dt, A_log, D, W_out)

    def _L0_ffn_ref(hidden_states, router_weight, router_bias, gate_up_proj, gate_up_proj_bias, down_proj, down_proj_bias):
        import jax, jax.numpy as jnp
        import numpy as np
        SWIGLU_ALPHA = 1.702
        SWIGLU_LIMIT = 7.0
        TOP_K = 4
        B, S, D = hidden_states.shape
        E = router_weight.shape[0]
        x = hidden_states.reshape(-1, D)
        N = x.shape[0]
        logits = x @ router_weight.T + router_bias
        topk_logits, topk_idx = jax.lax.top_k(logits, TOP_K)
        topk_w = jax.nn.softmax(topk_logits.astype(jnp.float32), axis=-1)
        combine = jnp.zeros((N, E), dtype=jnp.float32)
        combine = combine.at[jnp.arange(N)[:, None], topk_idx].set(topk_w)
        gate_up = jnp.einsum('nd,ejd->nej', x, gate_up_proj) + gate_up_proj_bias
        gate, up = jnp.split(gate_up, 2, axis=-1)
        gate = jnp.minimum(gate, SWIGLU_LIMIT)
        up = jnp.clip(up, -SWIGLU_LIMIT, SWIGLU_LIMIT)
        act = (up + 1.0) * gate * jax.nn.sigmoid(SWIGLU_ALPHA * gate)
        out = jnp.einsum('nei,edi->ned', act, down_proj) + down_proj_bias
        y = jnp.einsum('ned,ne->nd', out, combine.astype(out.dtype))
        return y.reshape(B, S, D)
    x = L0_attn_x
    x = x + _layernorm(_L0_attn_ref(_layernorm(x, axis=-1), L0_attn_ln_g, L0_attn_ln_b, L0_attn_W_in, L0_attn_conv_w, L0_attn_conv_b, L0_attn_W_xproj, L0_attn_W_dt, L0_attn_b_dt, L0_attn_A_log, L0_attn_D, L0_attn_W_out), axis=-1)
    x = x + _layernorm(_L0_ffn_ref(_layernorm(x, axis=-1), L0_ffn_router_weight, L0_ffn_router_bias, L0_ffn_gate_up_proj, L0_ffn_gate_up_proj_bias, L0_ffn_down_proj, L0_ffn_down_proj_bias), axis=-1)
    return x

_drawn_inputs = setup_inputs


def setup_inputs(seed=0):
    import zlib

    import numpy as np

    out = dict(_drawn_inputs(seed))
    spreads = {'L0_attn_ln_g': (1.0, 0.6),
     'L0_attn_ln_b': (0.0, 0.8),
     'L0_attn_conv_b': (0.0, 0.515),
     'L0_attn_D': (1.0, 0.6),
     'L0_ffn_router_bias': (0.0, 0.1),
     'L0_ffn_gate_up_proj_bias': (0.0, 0.1),
     'L0_ffn_down_proj_bias': (0.0, 0.1)}
    factors = {'L0_attn_W_in': 3.611,
     'L0_attn_conv_w': 3.792,
     'L0_attn_W_xproj': 8.0,
     'L0_attn_W_dt': 8.0,
     'L0_attn_b_dt': 8.0,
     'L0_attn_A_log': 8.0,
     'L0_attn_W_out': 3.44}
    for name, (base, spread) in spreads.items():
        noise = np.random.default_rng([zlib.crc32(name.encode()), seed]).standard_normal(out[name].shape)
        drawn = base * np.exp(spread * noise) if base else spread * noise
        out[name] = jnp.asarray(drawn.astype(out[name].dtype))
    for name, factor in factors.items():
        out[name] = (out[name] * factor).astype(out[name].dtype)
    return out
```

```python
import concourse.bass as bass
from concourse import mybir
from contextlib import ExitStack

F32 = mybir.dt.float32
F32R = mybir.dt.float32r
I32 = mybir.dt.int32
U32 = mybir.dt.uint32
ALU = mybir.AluOpType
ACT = mybir.ActivationFunctionType
AX = mybir.AxisListType

P = 128
BATCH, L, DM = 2, 4096, 256
TOK = BATCH * L
DI = 2 * DM
NS = 16
RANK = 16
TAPS = 4
KD = DM // P
KJ = DI // P
XD = RANK + 2 * NS
NB = TOK // P
CB = 8
CT = CB * P
NQ = NB // CB * NS
RB = 2 * CB
RH = RB + 2
RS = 32
EPS = 1e-5
E, TOPK, FF = 8, 4, 512
KF = FF // P
UT = 512
UB = UT // P
REGION = TOK + UT
NU = TOK * TOPK // UT + E - 1
LIMIT, ALPHA = 7.0, 1.702
HALO = TAPS - 1

LAG_CONV = 1
LAG_INNER = 2
LAG_SCAN = LAG_INNER + CB
LAG_BACK = LAG_SCAN + CB
LAG_ROUTE = LAG_BACK + 1


class Span:

    def __init__(self, i, lo, hi):
        self.i, self.lo, self.hi = i, lo, hi

    def __add__(self, n):
        return Span(self.i + n if n else self.i, self.lo + n, self.hi + n)

    def times(self, n):
        return Span(self.i * n, self.lo * n, self.hi * n)


def wait(eng, sem, at, f):
    if f(at.hi) <= 0:
        return
    assert f(at.lo) > 0, (sem, at.lo, f(at.lo))
    eng.wait_ge(sem, f(at.i))


def alone(eng, carrier):
    eng.sem_inc(carrier, 1)


def sandwich(nc, t, out, debug):
    ctx = ExitStack()
    with ctx:
        def sb(name, shape, dt=F32):
            return ctx.enter_context(nc.sbuf_tensor(name, shape, dt))

        def ps(name, shape, dt=F32):
            return ctx.enter_context(nc.psum_tensor(name, shape, dt))

        def sem(name):
            return ctx.enter_context(nc.semaphore(name))

        scan_b = nc.dram_tensor("scan_b", (NS, TOK), F32, kind="Internal").ap()
        x1_d = out if debug else nc.dram_tensor("x1_d", (TOK, DM), F32, kind="Internal").ap()
        xn_d = nc.dram_tensor("xn_d", (TOK, DM), F32, kind="Internal").ap()

        xs_d = nc.dram_tensor("xs_d", (E * REGION, DM), F32, kind="Internal").ap()
        ys_d = nc.dram_tensor("ys_d", (NU * UT, DM), F32, kind="Internal").ap()

        ident = sb("ident", [P, P])
        logits = sb("logits", [P, NB, E])
        mamba(nc, ctx, t, scan_b, x1_d, xn_d, logits, ident)
        place = sb("place", [P, NB, TOPK], I32)
        weight = sb("weight", [P, NB, TOPK])
        units = sb("units", [P, 2, NU], I32)
        with ExitStack() as lg:
            if not debug:
                w_gu = lg.enter_context(nc.sbuf_tensor("w_gu", [P, E, KD, 2 * FF], F32))
                w_dn = lg.enter_context(nc.sbuf_tensor("w_dn", [P, E, KF, DM], F32))
                route(nc, ctx, t, xn_d, xs_d, logits, place, weight, units, w_gu, w_dn)
                experts(nc, ctx, t, xs_d, ys_d, ident, units, w_gu, w_dn)
        if not debug:
            combine(nc, ctx, x1_d, ys_d, place, weight, out)


def mamba(nc, outer, t, scan_b, x1_d, xn_d, logits, ident):
    with ExitStack() as ctx:
        def sb(name, shape, dt=F32):
            return ctx.enter_context(nc.sbuf_tensor(name, shape, dt))

        def ps(name, shape, dt=F32):
            return ctx.enter_context(nc.psum_tensor(name, shape, dt))

        w_in = sb("w_in", [P, KD, 2 * DI])
        w_x = sb("w_x", [P, KJ, XD])
        w_dt = sb("w_dt", [RANK, DI])
        w_out = sb("w_out", [P, KJ, DM])
        w_r = sb("w_r", [P, KD, E])
        ln_gb = sb("ln_gb", [P, 2, KD])
        chan = sb("chan", [P, 3 + TAPS, KJ])
        rbias = sb("rbias", [P, E])
        a_neg = sb("a_neg", [P, KJ, NS])
        keep_eps = sb("keep_eps", [P, 1])
        ln_one = sb("ln_one", [P, 1])
        keep_chunk = sb("keep_chunk", [P, NB // CB])
        keep_block = sb("keep_block", [P, L // P])

        x_in = sb("x_in", [P, 2, DM])
        f_st = sb("f_st", [P, 6])
        f_agg = sb("f_agg", [P, 2])
        f_ln = sb("f_ln", [P, 4])
        f_rr = sb("f_rr", [P, 1])
        stat = sb("stat", [P, RS, 4])
        h0 = sb("h0", [P, DM])
        hT = sb("hT", [P, RH, KD, P])
        u_pre = sb("u_pre", [P, KJ, HALO + P])
        conv_acc = sb("conv_acc", [P, KJ, P])
        conv_tmp = sb("conv_tmp", [P, KJ, P])
        u_blk = sb("u_blk", [P, KJ, P])
        xd = sb("xd", [XD, P])
        c_ring = sb("c_ring", [P, RS, NS])
        dt_x = sb("dt_x", [P, KJ, P])
        dt_e = sb("dt_e", [P, KJ, P])
        dt_w = sb("dt_w", [P, KJ, P])
        dt_ring = sb("dt_ring", [P, KJ, RB * P])
        w_ring = sb("w_ring", [P, KJ, RB * P])
        b_rows = sb("b_rows", [P, 2, CT])
        dbu = sb("dbu", [P, KJ, CT])
        h = sb("h", [P, 2, KJ, CT])
        h_last = sb("h_last", [P, NS, KJ])
        y_acc = sb("y_acc", [P, RB, DI])
        x_again = sb("x_again", [P, DM])
        sz = sb("sz", [P, KJ, P])
        u_d = sz
        y_blk = sb("y_blk", [P, DI])
        ygT = sb("ygT", [P, KJ, P])
        xhat = sb("xhat", [P, DM])
        b_st = sb("b_st", [P, 12])
        b_mv = sb("b_mv", [P, 4])
        b_r = sb("b_r", [P, 4])
        x1 = sb("x1", [P, DM])
        xn = sb("xn", [P, DM])
        x2T = sb("x2T", [P, KD, P])

        p_da = ps("p_da", [P, 2, CT])
        p_ht = ps("p_ht", [P, 2, DI])
        p_f = ps("p_f", [P, DI])
        p_b = ps("p_b", [P, DI])

        names = """loaded consts_dve consts_pool a_exp consts
            sp_carrier dve_carrier pe_carrier x_loaded f_stats f_aggr f_mv f_lnv f_r1 f_v2 f_lnv2 f_r2 f_rr_s f_h0 xT_done hT_done
            up_done up_copied conv_first conv_m conv_a conv_done halo_done
            u_done xd_done xd_copied ct_done c_copied dt_done dtx_done dt_abs dt_exp dt_one dt_rest dt_ln dt_pos dt_ready w_ready
            ud_done udT_done y_init b_stored
            b_loaded dbu_done da_done scan_done last_done ht_done stt_done
            z_done sz_done y_copied yT_done yg_done xa_loaded xh_done o_done mo_done m_stats m_mv m_ln m_r
            x1n_done x1_done n_stats n_mv n_ln n_r xn_done x1_stored xn_stored
            x2T_done x2_copied lg_done lg_copied finished""".split()
        s = {n: outer.enter_context(nc.semaphore(n)) for n in names}

        def ring(at, depth):
            return at.i % depth

        def chunk_cols(q):
            return bass.ds((q.i // NS) % 2 * CT, CT)

        def slots(eng, body):
            T = NB
            cuts = [0, LAG_CONV, LAG_INNER, LAG_INNER + 1, LAG_SCAN, LAG_SCAN + 1, LAG_BACK, LAG_ROUTE, LAG_ROUTE + 1, T - 1, T, T + LAG_CONV, T + LAG_INNER,
                    T + LAG_SCAN - 1, T + LAG_SCAN, T + LAG_SCAN + 1, T + LAG_BACK - 1, T + LAG_BACK, T + LAG_ROUTE]
            for lo, hi in zip(cuts, cuts[1:]):
                run = {
                    "front": lo < T,
                    "conv": LAG_CONV <= lo < T + LAG_CONV,
                    "inner": LAG_INNER <= lo < T + LAG_INNER,
                    "scan": LAG_SCAN <= lo < T + LAG_SCAN,
                    "back": LAG_BACK <= lo < T + LAG_BACK,
                    "route": LAG_ROUTE <= lo < T + LAG_ROUTE,
                    "sum0": LAG_SCAN < lo < T + LAG_SCAN + 1,
                    "sum1": LAG_SCAN <= lo < T + LAG_SCAN,
                }
                pairs = (hi - lo) // 2
                if pairs > 1:
                    with eng.Fori(0, pairs) as i:
                        for v in (lo, lo + 1):
                            body(Span(i * 2 + v, v, v + 2 * (pairs - 1)), run)
                    lo += 2 * pairs
                for v in range(lo, hi):
                    body(Span(v, v, v), run)

        block = ctx.enter_context(nc.Block())

        @block.sync
        def _(eng):
            loads = [(w_in[:, :, :], t["w_in"]), (w_x[:, :, :], t["w_x"]), (w_dt[:, :], t["w_dt"]),
                     (w_out[:, :, :], t["w_out"]), (w_r[:, :, :], t["w_r"]), (ln_gb[:, :, :], t["ln_gb"]),
                     (chan[:, :, :], t["chan"]), (a_neg[:, :, :], t["a_log"]),
                     (rbias[:, :], t["rbias"].partition_broadcast(P))]
            for dst, src in loads:
                eng.dma_start(dst, src).then_inc(s["loaded"], 16)
            eng.wait_ge(s["loaded"], 16 * len(loads))

            def hold(sem, at, f):
                wait(eng, sem, at, f)
                alone(eng, s["sp_carrier"])

            def load_x(b):
                hold(s["x_loaded"], b, lambda i: 16 * i)
                hold(s["f_h0"], b, lambda i: i - 1)
                eng.dma_start(x_in[:, bass.ds(ring(b, 2), 1), :].rearrange("p a d -> p (a d)"),
                              t["x"][bass.ds(b.i * P, P), :]).then_inc(s["x_loaded"], 16)

            def store_b(b):
                hold(s["b_stored"], b, lambda i: 16 * i)
                hold(s["xd_copied"], b, lambda i: i + 1)
                eng.dma_start(scan_b[:, bass.ds(b.i * P, P)], xd[RANK:RANK + NS, :]).then_inc(s["b_stored"], 16)

            def load_b(q):
                hold(s["b_loaded"], q, lambda i: 16 * i)
                hold(s["b_stored"], q, lambda i: (i // NS + 1) * (16 * CB))
                hold(s["dbu_done"], q, lambda i: KJ * (i - 1))
                row = scan_b[bass.ds(q.i % NS, 1), bass.ds(q.i // NS * CT, CT)]
                eng.dma_start(b_rows[:, bass.ds(q.i % 2, 1), :].rearrange("p a d -> p (a d)"),
                              row.to_broadcast([P, CT])).then_inc(s["b_loaded"], 16)

            def load_again(b):
                hold(s["xa_loaded"], b, lambda i: 16 * i)
                hold(s["x1_done"], b, lambda i: i)
                eng.dma_start(x_again[:, :], t["x"][bass.ds(b.i * P, P), :]).then_inc(s["xa_loaded"], 16)

            def store_back(b):
                hold(s["x1_stored"], b, lambda i: 16 * i)
                hold(s["x1_done"], b, lambda i: i + 1)
                eng.dma_start(x1_d[bass.ds(b.i * P, P), :], x1[:, :]).then_inc(s["x1_stored"], 16)
                hold(s["xn_stored"], b, lambda i: 16 * i)
                hold(s["xn_done"], b, lambda i: i + 1)
                eng.dma_start(xn_d[bass.ds(b.i * P, P), :], xn[:, :]).then_inc(s["xn_stored"], 16)

            load_x(Span(0, 0, 0))

            def body(at, run):
                if run["front"] and at.hi < NB - 1:
                    load_x(at + 1)
                if run["scan"]:
                    if at.lo == LAG_SCAN:
                        load_b(Span(0, 0, 0))
                    load_b((at + -LAG_SCAN).times(2) + 1)
                if run["back"]:
                    load_again(at + -LAG_BACK)
                if run["inner"]:
                    store_b(at + -LAG_INNER)
                if run["scan"] and at.hi < NB + LAG_SCAN - 1:
                    load_b((at + -LAG_SCAN).times(2) + 2)
                if run["back"]:
                    store_back(at + -LAG_BACK)

            slots(eng, body)
            eng.wait_ge(s["b_stored"], 16 * NB)
            eng.wait_ge(s["x1_stored"], 16 * NB)
            eng.wait_ge(s["xn_stored"], 16 * NB)

        @block.gpsimd
        def _(eng):
            eng.memset(ident[:, :], 0.0).then_inc(s["consts_pool"], 1)
            eng.memset(u_pre[:, :, 0:HALO], 0.0).then_inc(s["consts_pool"], 1)
            eng.wait_ge(s["consts_pool"], 1)
            eng.affine_select(out=ident[:, :], in_=ident[:, :], compare_op=ALU.not_equal, fill=1.0,
                              base=0, pattern=[[-1, P]], channel_multiplier=1).then_inc(s["consts_pool"], 1)
            eng.wait_ge(s["loaded"], 16 * 9)
            eng.wait_ge(s["consts_dve"], 3)
            eng.wait_ge(s["consts_pool"], 3)

            def dbu_tile(q, j):
                if j == 0:
                    wait(eng, s["w_ready"], q, lambda i: (i // NS + 1) * CB)
                    wait(eng, s["b_loaded"], q, lambda i: 16 * (i + 1))
                wait(eng, s["scan_done"], q, lambda i: KJ * (i - 1) + j + 1)
                eng.tensor_tensor(dbu[:, j, :], w_ring[:, j, chunk_cols(q)],
                                  b_rows[:, bass.ds(ring(q, 2), 1), :].rearrange("p a d -> p (a d)"),
                                  ALU.mult).then_inc(s["dbu_done"], 1)

            def conv(b, k):
                if k == 0:
                    wait(eng, s["up_copied"], b, lambda i: i + 1)
                wait(eng, s["conv_a"], b, lambda i: HALO * i + k)
                eng.tensor_tensor(conv_tmp[:, :, :], u_pre[:, :, k:k + P],
                                  chan[:, 3 + k, :].unsqueeze(2).to_broadcast([P, KJ, P]),
                                  ALU.mult).then_inc(s["conv_m"], 1)
                wait(eng, s["conv_m"], b, lambda i: HALO * i + k + 1)
                if k == 0:
                    wait(eng, s["conv_first"], b, lambda i: i + 1)
                eng.tensor_tensor(conv_acc[:, :, :], conv_acc[:, :, :], conv_tmp[:, :, :],
                                  ALU.add).then_inc(s["conv_a"], 1)

            def dt_times_u(b):
                wait(eng, s["dbu_done"], b, lambda i: (i - CB) * 2 * KJ)
                wait(eng, s["dt_ready"], b, lambda i: i + 1)
                wait(eng, s["u_done"], b, lambda i: i + 1)
                eng.tensor_tensor(w_ring[:, :, bass.ds(ring(b, RB) * P, P)], dt_ring[:, :, bass.ds(ring(b, RB) * P, P)], u_blk[:, :, :],
                                  ALU.mult).then_inc(s["w_ready"], 1)

            def keep_halo(b):
                wait(eng, s["conv_a"], b, lambda i: HALO * (i + 1))
                eng.tensor_tensor(u_pre[:, :, 0:HALO], u_pre[:, :, P:P + HALO],
                                  keep_block[:, bass.ds(b.i % (L // P), 1)].unsqueeze(2).to_broadcast([P, KJ, HALO]),
                                  ALU.mult).then_inc(s["halo_done"], 1)

            def body(at, run):
                q = (at + -LAG_SCAN).times(2)
                taps = {(0, 2): 0, (0, 3): 1, (1, 0): 2}
                for half in range(2):
                    for j in range(KJ):
                        if run["scan"]:
                            dbu_tile(q + half, j)
                        if run["conv"] and (half, j) in taps:
                            conv(at + -LAG_CONV, taps[half, j])
                            if taps[half, j] == HALO - 1:
                                keep_halo(at + -LAG_CONV)
                        if run["inner"] and (half, j) == (1, 2):
                            dt_times_u(at + -LAG_INNER)

            slots(eng, body)

        @block.scalar
        def _(eng):
            eng.wait_ge(s["loaded"], 16 * 9)
            eng.activation(a_neg[:, :, :], a_neg[:, :, :], ACT.Exp).then_inc(s["a_exp"], 1)
            eng.wait_ge(s["consts_dve"], 4)
            eng.preload_act_table_set("natural_log_exp_and_others")
            eng.activation(ln_one[:, :], ln_one[:, :], ACT.Ln).then_inc(s["a_exp"], 1)

            def exp_da(q, j):
                if j == 0:
                    wait(eng, s["dt_ready"], q, lambda i: (i // NS + 1) * CB)
                wait(eng, s["scan_done"], q, lambda i: KJ * i + j - 1)
                a_nj = a_neg[:, j, bass.ds(q.i % NS, 1)]
                eng.activation(p_da[:, j % 2, :], dt_ring[:, j, chunk_cols(q)], ACT.Exp,
                               scale=a_nj).then_inc(s["da_done"], 1)

            def silus(at, run):
                if run["inner"]:
                    b = at + -LAG_INNER
                    wait(eng, s["conv_a"], b, lambda i: HALO * (i + 1))
                    wait(eng, s["w_ready"], b, lambda i: i)
                    wait(eng, s["xd_done"], b, lambda i: i)
                    wait(eng, s["ud_done"], b, lambda i: KJ * i)
                    eng.activation(u_blk[:, :, :], conv_acc[:, :, :], ACT.Silu).then_inc(s["u_done"], 1)
                if run["back"]:
                    b = at + -LAG_BACK
                    wait(eng, s["z_done"], b, lambda i: i + 1)
                    wait(eng, s["yg_done"], b, lambda i: i)
                    if run["inner"]:
                        wait(eng, s["udT_done"], at + -LAG_INNER, lambda i: i)
                    else:
                        eng.wait_ge(s["udT_done"], NB)
                    eng.activation(sz[:, :, :].rearrange("p j t -> p (j t)"), p_b[:, :], ACT.Silu).then_inc(s["sz_done"], 1)

            def rstd(src, ready, ln, ln_sem, dst, dst_sem, at, n=1):
                wait(eng, s[ready], at, lambda i: i + 1)
                eng.activation(ln, src, ACT.Ln, bias=keep_eps[:, 0:1]).then_inc(s[ln_sem], 1)
                wait(eng, s[ln_sem], at, lambda i: i + 1)
                eng.activation(dst, ln, ACT.Exp, scale=-0.5).then_inc(s[dst_sem], 1)

            def xd_copy(b):
                wait(eng, s["xd_done"], b, lambda i: i + 1)
                wait(eng, s["b_stored"], b, lambda i: 16 * i)
                wait(eng, s["dt_done"], b, lambda i: i)
                wait(eng, s["ct_done"], b, lambda i: i)
                eng.activation(xd[:, :], p_f[0:XD, 0:P], ACT.Copy).then_inc(s["xd_copied"], 1)

            def c_copy(b):
                wait(eng, s["ct_done"], b, lambda i: i + 1)
                eng.activation(c_ring[:, bass.ds(ring(b, RS), 1), :].rearrange("p a n -> p (a n)"),
                               p_f[:, RANK + NS:XD], ACT.Copy).then_inc(s["c_copied"], 1)

            def softplus(b):
                wait(eng, s["dtx_done"], b, lambda i: i + 1)
                wait(eng, s["dt_ready"], b, lambda i: i)
                eng.activation(dt_e[:, :, :], dt_x[:, :, :], ACT.Abs).then_inc(s["dt_abs"], 1)
                wait(eng, s["dt_abs"], b, lambda i: i + 1)
                eng.activation(dt_e[:, :, :], dt_e[:, :, :], ACT.Exp, scale=-1.0).then_inc(s["dt_exp"], 1)
                wait(eng, s["dt_exp"], b, lambda i: i + 1)
                eng.activation(dt_w[:, :, :], dt_e[:, :, :], ACT.Identity, bias=1.0).then_inc(s["dt_one"], 1)

            def softplus_ln(b):
                wait(eng, s["dt_rest"], b, lambda i: i + 1)
                eng.activation(dt_w[:, :, :], dt_w[:, :, :], ACT.Ln).then_inc(s["dt_ln"], 1)

            def h_copy(b):
                wait(eng, s["xT_done"], b, lambda i: i + 1)
                wait(eng, s["z_done"], b, lambda i: i - RH + 1)
                for k in range(KD):
                    eng.activation(hT[:, bass.ds(ring(b, RH), 1), k, :].rearrange("p a t -> p (a t)"),
                                   p_f[:, k * P:(k + 1) * P], ACT.Identity,
                                   bias=ln_gb[:, 1, k:k + 1], scale=ln_gb[:, 0, k:k + 1]).then_inc(s["hT_done"], 1)

            def u_copy(b):
                wait(eng, s["up_done"], b, lambda i: i + 1)
                wait(eng, s["halo_done"], b, lambda i: i)
                eng.activation(u_pre[:, :, HALO:HALO + P], p_f[:, :].rearrange("p (j t) -> p j t", j=KJ),
                               ACT.Copy).then_inc(s["up_copied"], 1)
                wait(eng, s["u_done"], b, lambda i: i)
                for j in range(KJ):
                    last = eng.activation(conv_acc[:, j, :], p_f[:, j * P:(j + 1) * P], ACT.Identity,
                                          bias=chan[:, 0, j:j + 1], scale=chan[:, 3 + HALO, j:j + 1])
                last.then_inc(s["conv_first"], 1)

            def u_times_d(b, back):
                wait(eng, s["udT_done"], b, lambda i: i)
                if back:
                    wait(eng, s["yg_done"], back, lambda i: i + 1)
                wait(eng, s["u_done"], b, lambda i: i + 1)
                for j in range(KJ):
                    eng.activation(u_d[:, j, :], u_blk[:, j, :], ACT.Copy,
                                   scale=chan[:, 1, j:j + 1]).then_inc(s["ud_done"], 1)

            def y_start(b):
                wait(eng, s["udT_done"], b, lambda i: i + 1)
                wait(eng, s["y_copied"], b, lambda i: i - RB + 1)
                eng.activation(y_acc[:, bass.ds(ring(b, RB), 1), :].rearrange("p a d -> p (a d)"),
                               p_f[:, :], ACT.Copy).then_inc(s["y_init"], 1)

            def y_copy(b):
                wait(eng, s["stt_done"], b, lambda i: (i // CB) * (CB * NS) + (NS - 1) * CB + i % CB + 1)
                wait(eng, s["yT_done"], b, lambda i: i)
                eng.activation(y_blk[:, :], y_acc[:, bass.ds(ring(b, RB), 1), :].rearrange("p a d -> p (a d)"),
                               ACT.Copy).then_inc(s["y_copied"], 1)

            def x2_copy(b):
                wait(eng, s["x2T_done"], b, lambda i: i + 1)
                eng.activation(x2T[:, :, :].rearrange("p k t -> p (k t)"), p_f[:, DM:2 * DM], ACT.Copy).then_inc(s["x2_copied"], 1)

            def stat_col(b, c):
                return stat[:, bass.ds(ring(b, RS), 1), c:c + 1].rearrange("p a c -> p (a c)")

            def body(at, run):
                q = (at + -LAG_SCAN).times(2)
                inner, back, route = at + -LAG_INNER, at + -LAG_BACK, at + -LAG_ROUTE
                scan = run["scan"]
                if scan:
                    exp_da(q, 0)
                silus(at, run)
                if run["inner"] or run["back"]:
                    eng.preload_act_table_set("natural_log_exp_and_others")
                if scan:
                    exp_da(q, 1)
                if run["back"]:
                    y_copy(back)
                if run["conv"]:
                    u_copy(at + -LAG_CONV)
                if scan:
                    exp_da(q, 2)
                if run["inner"]:
                    xd_copy(inner)
                if run["front"]:
                    rstd(stat_col(at, 1), "f_mv", f_ln[:, 0:1], "f_lnv", stat_col(at, 2), "f_r1", at)
                if run["inner"]:
                    c_copy(inner)
                if scan:
                    exp_da(q, 3)
                if run["inner"]:
                    u_times_d(inner, back if run["back"] else None)
                    softplus(inner)
                if scan:
                    exp_da(q + 1, 0)
                if run["front"]:
                    rstd(f_ln[:, 1:2], "f_v2", f_ln[:, 2:3], "f_lnv2", f_ln[:, 3:4], "f_r2", at)
                if run["inner"]:
                    softplus_ln(inner)
                if scan:
                    exp_da(q + 1, 1)
                if run["inner"]:
                    y_start(inner)
                if scan:
                    exp_da(q + 1, 2)
                if run["back"]:
                    rstd(b_mv[:, 1:2], "m_mv", b_r[:, 0:1], "m_ln", b_r[:, 1:2], "m_r", back)
                if scan:
                    exp_da(q + 1, 3)
                if run["front"]:
                    h_copy(at)
                if run["route"]:
                    x2_copy(route)
                if run["back"]:
                    rstd(b_mv[:, 3:4], "n_mv", b_r[:, 2:3], "n_ln", b_r[:, 3:4], "n_r", back)

            slots(eng, body)

        @block.vector
        def _(eng):
            eng.memset(keep_chunk[:, :], 1.0)
            eng.memset(keep_block[:, :], 1.0)
            eng.memset(keep_eps[:, :], EPS)
            eng.memset(ln_one[:, :], 1.0)
            eng.memset(h_last[:, :, :], 0.0).then_inc(s["consts_dve"], 1)
            eng.wait_ge(s["consts_dve"], 1)
            eng.memset(keep_chunk[:, L // CT - 1::L // CT], 0.0).then_inc(s["consts_dve"], 1)
            eng.memset(keep_block[:, L // P - 1:L // P], 0.0).then_inc(s["consts_dve"], 1)
            eng.wait_ge(s["a_exp"], 1)
            eng.tensor_scalar(a_neg[:, :, :], a_neg[:, :, :], -1.0, None, ALU.mult).then_inc(s["consts_dve"], 1)

            def stat_col(b, c, n=1):
                return stat[:, bass.ds(ring(b, RS), 1), c:c + n].rearrange("p a c -> p (a c)")

            def x_of(b):
                return x_in[:, bass.ds(ring(b, 2), 1), :].rearrange("p a d -> p (a d)")

            def front_stats(b):
                wait(eng, s["x_loaded"], b, lambda i: 16 * (i + 1))
                eng.bn_stats(f_st[:, :], x_of(b)).then_inc(s["f_stats"], 1)

            def front_aggr(b):
                wait(eng, s["f_stats"], b, lambda i: i + 1)
                alone(eng, s["dve_carrier"])
                eng.bn_aggr(f_agg[:, :], f_st[:, :]).then_inc(s["f_aggr"], 1)

            def front_keep(b):
                wait(eng, s["f_aggr"], b, lambda i: i + 1)
                eng.tensor_copy(stat_col(b, 0, 2), f_agg[:, :]).then_inc(s["f_mv"], 1)

            def front_var(b):
                wait(eng, s["f_r1"], b, lambda i: i + 1)
                eng.tensor_scalar(f_ln[:, 1:2], stat_col(b, 1), stat_col(b, 2), stat_col(b, 2),
                                  ALU.mult, ALU.mult).then_inc(s["f_v2"], 1)

            def front_norm(b):
                wait(eng, s["f_r2"], b, lambda i: i + 1)
                eng.tensor_tensor(f_rr[:, :], stat_col(b, 2), f_ln[:, 3:4], ALU.mult).then_inc(s["f_rr_s"], 1)
                wait(eng, s["f_rr_s"], b, lambda i: i + 1)
                wait(eng, s["xT_done"], b, lambda i: i)
                eng.tensor_scalar(h0[:, :], x_of(b), stat_col(b, 0), f_rr[:, 0:1],
                                  ALU.subtract, ALU.mult).then_inc(s["f_h0"], 1)

            def dt_bias(b):
                wait(eng, s["dt_done"], b, lambda i: i + 1)
                eng.tensor_tensor(dt_x[:, :, :], p_f[:, :].rearrange("p (j t) -> p j t", j=KJ),
                                  chan[:, 2, :].unsqueeze(2).to_broadcast([P, KJ, P]),
                                  ALU.add).then_inc(s["dtx_done"], 1)

            def ring_cols(b):
                return bass.ds(ring(b, RB) * P, P)

            def dt_rest(b):
                wait(eng, s["dt_one"], b, lambda i: i + 1)
                eng.scalar_tensor_tensor(out=dt_e[:, :, :], in0=dt_w[:, :, :], scalar=1.0, in1=dt_e[:, :, :],
                                         op0=ALU.subtract, op1=ALU.subtract).then_inc(s["dt_rest"], 1)

            def dt_finish(b):
                wait(eng, s["dt_ln"], b, lambda i: i + 1)
                wait(eng, s["scan_done"], b, lambda i: (i - CB) * 2 * KJ)
                eng.scalar_tensor_tensor(out=dt_x[:, :, :], in0=dt_x[:, :, :], scalar=0.0,
                                         in1=dt_w[:, :, :], op0=ALU.max, op1=ALU.add).then_inc(s["dt_pos"], 1)

            def dt_keep(b):
                wait(eng, s["dt_pos"], b, lambda i: i + 1)
                eng.scalar_tensor_tensor(out=dt_ring[:, :, ring_cols(b)], in0=dt_x[:, :, :], scalar=ln_one[:, 0:1],
                                         in1=dt_e[:, :, :], op0=ALU.subtract, op1=ALU.subtract)\
                   .then_inc(s["dt_ready"], 1)

            def scan(q, half, j):
                wait(eng, s["da_done"], q, lambda i: KJ * i + j + 1)
                wait(eng, s["dbu_done"], q, lambda i: KJ * i + j + 1)
                wait(eng, s["ht_done"], q, lambda i: CB * (i - 1))
                wait(eng, s["last_done"], q, lambda i: i - NS + 1)
                eng.tensor_tensor_scan(h[:, half, j, :], p_da[:, j % 2, :], dbu[:, j, :],
                                       h_last[:, bass.ds(q.i % NS, 1), j:j + 1].rearrange("p a c -> p (a c)"),
                                       ALU.mult, ALU.add).then_inc(s["scan_done"], 1)

            def keep_last(q, half):
                wait(eng, s["scan_done"], q, lambda i: KJ * (i + 1))
                eng.tensor_scalar(h_last[:, bass.ds(q.i % NS, 1), :].rearrange("p a j -> p (a j)"),
                                  h[:, half, :, CT - 1], keep_chunk[:, bass.ds(q.i // NS, 1)], None,
                                  ALU.mult).then_inc(s["last_done"], 1)

            def add_state(q, g):
                blk = q.i // NS * CB + g
                if g == 0:
                    wait(eng, s["y_init"], q, lambda i: (i // NS + 1) * CB)
                    wait(eng, s["c_copied"], q, lambda i: (i // NS + 1) * CB)
                wait(eng, s["stt_done"], q, lambda i: CB * (i - 1) + g + 1)
                y = y_acc[:, bass.ds(blk % RB, 1), :].rearrange("p a d -> p (a d)")
                c = c_ring[:, bass.ds(blk % RS, 1), bass.ds(q.i % NS, 1)].rearrange("p a c -> p (a c)")
                wait(eng, s["ht_done"], q, lambda i: CB * i + g + 1)
                eng.scalar_tensor_tensor(out=y, in0=p_ht[:, g % 2, :], scalar=c, in1=y,
                                         op0=ALU.mult, op1=ALU.add).then_inc(s["stt_done"], 1)

            def gate(b):
                wait(eng, s["yT_done"], b, lambda i: i + 1)
                wait(eng, s["sz_done"], b, lambda i: i + 1)
                wait(eng, s["o_done"], b, lambda i: i)
                eng.tensor_tensor(ygT[:, :, :].rearrange("p j t -> p (j t)"), p_b[:, :],
                                  sz[:, :, :].rearrange("p j t -> p (j t)"), ALU.mult).then_inc(s["yg_done"], 1)
                wait(eng, s["xa_loaded"], b, lambda i: 16 * (i + 1))
                eng.tensor_scalar(xhat[:, :], x_again[:, :], stat_col(b, 0), stat_col(b, 2),
                                  ALU.subtract, ALU.mult).then_inc(s["xh_done"], 1)

            def mamba_out(b):
                wait(eng, s["o_done"], b, lambda i: i + 1)
                wait(eng, s["xh_done"], b, lambda i: i + 1)
                eng.tensor_tensor(xhat[:, :], p_b[:, 0:DM], xhat[:, :], ALU.add).then_inc(s["mo_done"], 1)

            def m_stats(b):
                wait(eng, s["mo_done"], b, lambda i: i + 1)
                eng.bn_stats(b_st[:, 0:6], xhat[:, :]).then_inc(s["m_stats"], 1)

            def m_aggr(b):
                wait(eng, s["m_stats"], b, lambda i: i + 1)
                alone(eng, s["dve_carrier"])
                eng.bn_aggr(b_mv[:, 0:2], b_st[:, 0:6]).then_inc(s["m_mv"], 1)

            def m_norm(b):
                wait(eng, s["m_r"], b, lambda i: i + 1)
                eng.tensor_scalar(xhat[:, :], xhat[:, :], b_mv[:, 0:1], b_r[:, 1:2],
                                  ALU.subtract, ALU.mult).then_inc(s["x1n_done"], 1)

            def residual(b):
                wait(eng, s["x1n_done"], b, lambda i: i + 1)
                wait(eng, s["x1_stored"], b, lambda i: 16 * i)
                eng.tensor_tensor(x1[:, :], xhat[:, :], x_again[:, :], ALU.add).then_inc(s["x1_done"], 1)

            def n_stats(b):
                wait(eng, s["x1_done"], b, lambda i: i + 1)
                eng.bn_stats(b_st[:, 6:12], x1[:, :]).then_inc(s["n_stats"], 1)

            def n_aggr(b):
                wait(eng, s["n_stats"], b, lambda i: i + 1)
                alone(eng, s["dve_carrier"])
                eng.bn_aggr(b_mv[:, 2:4], b_st[:, 6:12]).then_inc(s["n_mv"], 1)

            def norm2(b):
                wait(eng, s["n_r"], b, lambda i: i + 1)
                wait(eng, s["x2T_done"], b, lambda i: i)
                wait(eng, s["xn_stored"], b, lambda i: 16 * i)
                eng.tensor_scalar(xn[:, :], x1[:, :], b_mv[:, 2:3], b_r[:, 3:4],
                                  ALU.subtract, ALU.mult).then_inc(s["xn_done"], 1)

            def route(b):
                wait(eng, s["lg_done"], b, lambda i: i + 1)
                eng.tensor_tensor(logits[:, bass.ds(b.i, 1), :].rearrange("p a e -> p (a e)"), p_f[:, DM:DM + E],
                                  rbias[:, :], ALU.add).then_inc(s["lg_copied"], 1)

            FRONT = {(1, 0): [front_stats], (2, 0): [front_aggr], (3, 1): [front_keep], (7, 1): [front_var],
                     (10, 0): [front_norm]}
            INNER = {(7, 1): [dt_bias], (9, 0): [dt_rest], (10, 0): [dt_finish], (11, 0): [dt_keep]}
            BACK = {(4, 0): [gate], (11, 0): [mamba_out], (11, 1): [m_stats], (12, 0): [m_aggr], (13, 0): [m_norm],
                    (13, 1): [residual], (14, 0): [n_stats], (15, 0): [n_aggr], (15, 1): [norm2]}
            ROUTE = {(15, 1): [route]}

            def body(at, run):
                inner, back = at + -LAG_INNER, at + -LAG_BACK
                for half in range(2):
                    q = (at + -LAG_SCAN).times(2) + half
                    for g in range(CB):
                        G = half * CB + g
                        if run["sum1" if half else "sum0"]:
                            add_state(q + -1, g)
                        if run["sum1" if half else "sum0"] and g == 0:
                            keep_last(q + -1, 1 - half)
                        for stage, index, steps in (("front", at, FRONT), ("inner", inner, INNER),
                                                    ("back", back, BACK), ("route", at + -LAG_ROUTE, ROUTE)):
                            if run[stage] and (G, 0) in steps:
                                for step in steps[G, 0]:
                                    step(index)
                        if run["scan"] and g % 2:
                            scan(q, half, g // 2)
                        for stage, index, steps in (("front", at, FRONT), ("inner", inner, INNER),
                                                    ("back", back, BACK), ("route", at + -LAG_ROUTE, ROUTE)):
                            if run[stage] and (G, 1) in steps:
                                for step in steps[G, 1]:
                                    step(index)

            slots(eng, body)

        @block.tensor
        def _(eng):
            eng.wait_ge(s["loaded"], 16 * 9)
            eng.wait_ge(s["consts_pool"], 3)

            def turn_states(q, half, g):
                if g == 0:
                    wait(eng, s["scan_done"], q, lambda i: KJ * (i + 1))
                wait(eng, s["stt_done"], q, lambda i: CB * i + g - 1)
                for j in range(KJ):
                    mm = eng.transpose(p_ht[:, g % 2, j * P:(j + 1) * P], h[:, half, j, g * P:(g + 1) * P], ident[:, :])
                mm.then_inc(s["ht_done"], 1)

            def project_z(b, tiles, last):
                wait(eng, s["mo_done"], b, lambda i: i)
                wait(eng, s["hT_done"], b, lambda i: KD * (i + 1))
                for j in tiles:
                    for k in range(KD):
                        mm = eng.matmul(p_b[:, j * P:(j + 1) * P], w_in[:, k, DI + j * P:DI + (j + 1) * P],
                                        hT[:, bass.ds(ring(b, RH), 1), k, :].rearrange("p a t -> p (a t)"),
                                        start=(k == 0), stop=(k == KD - 1))
                if last:
                    mm.then_inc(s["z_done"], 1)

            def turn_x(b, inner, before):
                wait(eng, s["f_h0"], b, lambda i: i + 1)
                if inner:
                    wait(eng, s["y_init"], inner, lambda i: i + 1)
                elif before:
                    wait(eng, s["conv_first"], before, lambda i: i + 1)
                for k in range(KD):
                    mm = eng.transpose(p_f[:, k * P:(k + 1) * P], h0[:, k * P:(k + 1) * P], ident[:, :])
                mm.then_inc(s["xT_done"], 1)

            def project_u(b, tiles, last, routed):
                wait(eng, s["hT_done"], b, lambda i: KD * (i + 1))
                if routed:
                    wait(eng, s["lg_copied"], routed, lambda i: i + 1)
                for j in tiles:
                    for k in range(KD):
                        mm = eng.matmul(p_f[:, j * P:(j + 1) * P], w_in[:, k, j * P:(j + 1) * P],
                                        hT[:, bass.ds(ring(b, RH), 1), k, :].rearrange("p a t -> p (a t)"),
                                        start=(k == 0), stop=(k == KD - 1))
                if last:
                    mm.then_inc(s["up_done"], 1)

            def project_xd(b, after):
                wait(eng, s["u_done"], b, lambda i: i + 1)
                if after:
                    wait(eng, s["conv_first"], after, lambda i: i + 1)
                else:
                    wait(eng, s["y_init"], b, lambda i: i)
                for j in range(KJ):
                    mm = eng.matmul(p_f[0:XD, 0:P], w_x[:, j, :], u_blk[:, j, :], start=(j == 0), stop=(j == KJ - 1))
                mm.then_inc(s["xd_done"], 1)

            def turn_c(b):
                wait(eng, s["xd_copied"], b, lambda i: i + 1)
                alone(eng, s["pe_carrier"])
                eng.transpose(p_f[:, 0:XD], xd[:, :], ident[0:XD, 0:XD]).then_inc(s["ct_done"], 1)

            def project_dt(b):
                wait(eng, s["c_copied"], b, lambda i: i + 1)
                for j in range(KJ):
                    mm = eng.matmul(p_f[:, j * P:(j + 1) * P], w_dt[:, j * P:(j + 1) * P], xd[0:RANK, :],
                                    start=True, stop=True)
                mm.then_inc(s["dt_done"], 1)

            def turn_ud(b):
                wait(eng, s["ud_done"], b, lambda i: KJ * (i + 1))
                wait(eng, s["dtx_done"], b, lambda i: i + 1)
                for j in range(KJ):
                    mm = eng.transpose(p_f[:, j * P:(j + 1) * P], u_d[:, j, :], ident[:, :])
                mm.then_inc(s["udT_done"], 1)

            def turn_y(b):
                wait(eng, s["sz_done"], b, lambda i: i + 1)
                wait(eng, s["y_copied"], b, lambda i: i + 1)
                for j in range(KJ):
                    mm = eng.transpose(p_b[:, j * P:(j + 1) * P], y_blk[:, j * P:(j + 1) * P], ident[:, :])
                mm.then_inc(s["yT_done"], 1)

            def project_out(b, tiles, last):
                wait(eng, s["yg_done"], b, lambda i: i + 1)
                for j in tiles:
                    mm = eng.matmul(p_b[:, 0:DM], ygT[:, j, :], w_out[:, j, :], start=(j == 0), stop=(j == KJ - 1))
                if last:
                    mm.then_inc(s["o_done"], 1)

            def turn_x2(b, inner):
                wait(eng, s["xn_done"], b, lambda i: i + 1)
                wait(eng, s["lg_copied"], b, lambda i: i)
                wait(eng, s["y_init"], inner, lambda i: i + 1)
                for k in range(KD):
                    mm = eng.transpose(p_f[:, DM + k * P:DM + (k + 1) * P], xn[:, k * P:(k + 1) * P], ident[:, :])
                mm.then_inc(s["x2T_done"], 1)

            def route(b):
                wait(eng, s["x2_copied"], b, lambda i: i + 1)
                for k in range(KD):
                    mm = eng.matmul(p_f[:, DM:DM + E], x2T[:, k, :], w_r[:, k, :], start=(k == 0), stop=(k == KD - 1))
                mm.then_inc(s["lg_done"], 1)

            def body(at, run):
                conv, inner, back, rt = at + -LAG_CONV, at + -LAG_INNER, at + -LAG_BACK, at + -LAG_ROUTE
                for half in range(2):
                    q = (at + -LAG_SCAN).times(2) + half
                    for g in range(CB):
                        G = half * CB + g
                        if run["sum1" if half else "sum0"]:
                            turn_states(q + -1, 1 - half, g)
                        if run["back"] and at.lo == LAG_BACK and G == 0:
                            project_z(back, range(KJ), True)
                        if run["conv"]:
                            routed = rt + -1 if rt.lo > 0 else None
                            if G in (0, 1):
                                project_u(conv, (G,), False, routed)
                            if G == 2:
                                project_u(conv, (2, 3), True, routed)
                        if run["inner"]:
                            if G == 4:
                                project_xd(inner, conv if run["conv"] else None)
                            if G == 5:
                                turn_c(inner)
                            if G == 6:
                                project_dt(inner)
                            if G == 11:
                                turn_ud(inner)
                        if run["route"]:
                            if G == 13:
                                turn_x2(rt, inner if run["inner"] else Span(NB - 1, NB - 1, NB - 1))
                        if run["front"] and G == 13:
                            turn_x(at, inner if run["inner"] else None, conv if run["conv"] else None)
                        if run["route"]:
                            if G == 15:
                                route(rt)
                        if run["back"]:
                            if G == 3:
                                turn_y(back)
                            if 7 <= G < 7 + KJ:
                                project_out(back, (G - 7,), G == 6 + KJ)
                            if at.hi < NB - 1 + LAG_BACK:
                                if G in (12, 14):
                                    project_z(back + 1, (G // 2 - 6,), False)
                                if G == 15:
                                    project_z(back + 1, (2, 3), True)

            slots(eng, body)


def route(nc, outer, t, xn_d, xs_d, logits, place, weight, units, w_gu, w_dn):
    with ExitStack() as ctx:
        def sb(name, shape, dt=F32):
            return ctx.enter_context(nc.sbuf_tensor(name, shape, dt))

        p_rank = ctx.enter_context(nc.psum_tensor("p_rank", [P, NB, E], F32))
        p_total = ctx.enter_context(nc.psum_tensor("p_total", [P, NB, E], F32))
        left = sb("left", [P, NB, E])
        best = sb("best", [P, TOPK, NB])
        choice = sb("choice", [P, TOPK, NB])
        top = sb("top", [P, NB, TOPK])
        top_sum = sb("top_sum", [P, NB])
        is_k = sb("is_k", [P, TOPK, NB, E])
        taken = sb("taken", [P, NB, E])
        below = sb("below", [P, P])
        ones = sb("ones", [P, P])
        expert_i = sb("expert_i", [P, E])
        expert_neg = sb("expert_neg", [P, E])
        size_i = sb("size_i", [P, TOK // UT])
        unit_i = sb("unit_i", [P, NU])
        same_e = sb("same_e", [P, E, NB])
        total = sb("total", [P, E, NB])
        upto = sb("upto", [P, E, NB])
        rank = sb("rank", [P, E, NB])
        base = sb("base", [P, E, NB])
        region = sb("region", [P, E])
        start_row = sb("start_row", [P, E])
        place_in = sb("place_in", [P, NB, TOPK], I32)
        hit = sb("hit", [P, NB, E])
        place_f = sb("place_f", [P, TOPK, NB])
        over = sb("over", [P, E, TOK // UT])
        n_units = sb("n_units", [P, E])
        unit_end = sb("unit_end", [P, E])
        last_unit = sb("last_unit", [P, 1])
        skip = sb("skip", [P, E])
        past = sb("past", [P, NU, E])
        past_skip = sb("past_skip", [P, NU, E])
        unit_f = sb("unit_f", [P, 3, NU])
        tail_f = sb("tail_f", [P, E])
        tail = sb("tail", [P, E], I32)
        zeros = sb("zeros", [P, UB, DM])
        rows = sb("rows", [P, 2, DM])
        place_now = sb("place_now", [P, 2, TOPK], I32)

        names = """r_const r_carrier r_zero r_iota r_taken r_counted r_step r_expin r_exp
            r_now in_ready place_ready unit_ready rows_loaded scat0 scat1 scat2 scat3 tails_stored wgu_loaded wdn_loaded""".split()
        s = {n: outer.enter_context(nc.semaphore(n)) for n in names}
        scat = [s[f"scat{k}"] for k in range(TOPK)]
        block = ctx.enter_context(nc.Block())

        @block.sync
        def _(eng):
            for e in range(E):
                if e >= E // 2:
                    eng.wait_ge(scat[0], 16 * (e - E // 2 + 1) * E)
                if e:
                    eng.wait_ge(s["wgu_loaded"], 16 * e)
                    eng.wait_ge(s["wdn_loaded"], 16 * e)
                eng.dma_start(w_gu[:, e], t["w_gu"][e].rearrange("(k p) f -> p k f", p=P)).then_inc(s["wgu_loaded"], 16)
                eng.dma_start(w_dn[:, e], t["w_dn"][e].rearrange("(k p) d -> p k d", p=P)).then_inc(s["wdn_loaded"], 16)
            eng.wait_ge(s["wgu_loaded"], 16 * E)
            eng.wait_ge(s["wdn_loaded"], 16 * E)
            eng.wait_ge(s["unit_ready"], 3)
            eng.wait_ge(s["r_zero"], 1)
            for e in range(E):
                first = eng.value_load(tail[0:1, e:e + 1], min_val=0, max_val=E * REGION - UT)
                eng.dma_start(xs_d[bass.ds(first, UT), :].rearrange("(t p) d -> p t d", p=P),
                              zeros[:, :, :]).then_inc(s["tails_stored"], 16)
            eng.wait_ge(s["tails_stored"], 16 * E)

        @block.gpsimd
        def _(eng):
            eng.memset(zeros[:, :, :], 0.0).then_inc(s["r_zero"], 1)
            eng.memset(ones[:, :], 1.0).then_inc(s["r_const"], 1)
            eng.wait_ge(s["r_const"], 1)
            eng.affine_select(out=below[:, :], in_=ones[:, :], compare_op=ALU.is_gt, fill=0.0, base=0,
                              pattern=[[1, P]], channel_multiplier=-1).then_inc(s["r_const"], 1)
            eng.iota(expert_i[:, :], pattern=[[1, E]], base=0, channel_multiplier=0,
                     allow_small_or_imprecise_dtypes=True).then_inc(s["r_iota"], 1)
            eng.iota(size_i[:, :], pattern=[[UT, TOK // UT]], base=0, channel_multiplier=0,
                     allow_small_or_imprecise_dtypes=True).then_inc(s["r_iota"], 1)
            eng.iota(unit_i[:, :], pattern=[[1, NU]], base=0, channel_multiplier=0,
                     allow_small_or_imprecise_dtypes=True).then_inc(s["r_iota"], 1)
            def scatter(b, half):
                wait(eng, s["rows_loaded"], b, lambda i: 16 * (i + 1))
                wait(eng, s["r_now"], b, lambda i: i + 1)
                for k in range(TOPK):
                    wait(eng, scat[k], b, lambda i: 16 * i)
                    alone(eng, s["r_carrier"])
                    eng.indirect_dma_start(
                        out=xs_d, out_offset=bass.IndirectOffsetOnAxis(ap=place_now[:, half, k:k + 1], axis=0),
                        in_=rows[:, half, :], in_offset=None,
                    ).then_inc(scat[k], 16)

            for half in range(2):
                scatter(Span(half, half, half), half)
            with eng.Fori(1, NB // 2) as i:
                for half in range(2):
                    scatter(Span(i * 2 + half, 2 + half, NB - 2 + half), half)
            for k in range(TOPK):
                eng.wait_ge(scat[k], 16 * NB)

        @block.scalar
        def _(eng):
            eng.wait_ge(s["r_expin"], 1)
            eng.activation(top[:, :, :], top[:, :, :], ACT.Exp).then_inc(s["r_exp"], 1)

            def load(b, half):
                wait(eng, s["rows_loaded"], b, lambda i: 16 * i)
                for k in range(TOPK):
                    wait(eng, scat[k], b, lambda i: 16 * (i - 1))
                eng.activation(place_now[:, half, :], place_in[:, bass.ds(b.i, 1), :].rearrange("p a k -> p (a k)"),
                               ACT.Copy).then_inc(s["r_now"], 1)
                eng.dma_start(rows[:, half, :], xn_d[bass.ds(b.i * P, P), :]).then_inc(s["rows_loaded"], 16)

            eng.wait_ge(s["in_ready"], TOPK)
            for v in range(2):
                load(Span(v, v, v), v)
            with eng.Fori(1, NB // 2) as i:
                for half in range(2):
                    load(Span(i * 2 + half, 2 + half, NB - 2 + half), half)

        @block.tensor
        def _(eng):
            eng.wait_ge(s["r_const"], 2)
            eng.wait_ge(s["r_taken"], TOPK)
            flat = taken[:, :, :].rearrange("p b e -> p (b e)")
            eng.matmul(p_rank[:, :, :].rearrange("p b e -> p (b e)"), below[:, :], flat, start=True, stop=True)
            eng.matmul(p_total[:, :, :].rearrange("p b e -> p (b e)"), ones[:, :], flat,
                       start=True, stop=True).then_inc(s["r_counted"], 1)

        @block.vector
        def _(eng):
            done = [0]

            def step(instruction):
                done[0] += 1
                instruction.then_inc(s["r_step"], 1)
                eng.wait_ge(s["r_step"], done[0])

            step(eng.memset(same_e[:, :, :], 1.0))
            step(eng.memset(same_e[:, :, 0:1], 0.0))
            eng.wait_ge(s["r_iota"], 3)
            step(eng.tensor_scalar(expert_neg[:, :], expert_i[:, :], float(E), None, ALU.subtract))
            step(eng.tensor_copy(left[:, :, :], logits[:, :, :]))
            for k in range(TOPK):
                step(eng.tensor_reduce(best[:, k, :], left[:, :, :], axis=AX.X, op=ALU.max))
                step(eng.tensor_tensor(hit[:, :, :], left[:, :, :], best[:, k, :].unsqueeze(2).to_broadcast([P, NB, E]),
                                       ALU.is_equal))
                step(eng.scalar_tensor_tensor(out=hit[:, :, :], in0=hit[:, :, :], scalar=float(-E),
                                              in1=expert_i[:, :].unsqueeze(1).to_broadcast([P, NB, E]),
                                              op0=ALU.mult, op1=ALU.add))
                step(eng.tensor_reduce(choice[:, k, :], hit[:, :, :], axis=AX.X, op=ALU.min))
                step(eng.tensor_tensor(is_k[:, k], choice[:, k, :].unsqueeze(2).to_broadcast([P, NB, E]),
                                       expert_neg[:, :].unsqueeze(1).to_broadcast([P, NB, E]), ALU.is_equal))
                if k < TOPK - 1:
                    step(eng.scalar_tensor_tensor(out=left[:, :, :], in0=is_k[:, k], scalar=-3e38, in1=left[:, :, :],
                                                  op0=ALU.mult, op1=ALU.add))
            eng.tensor_tensor(top[:, :, :].rearrange("p b k -> p k b"), best[:, :, :],
                              best[:, 0:1, :].to_broadcast([P, TOPK, NB]), ALU.subtract).then_inc(s["r_expin"], 1)
            eng.tensor_copy(taken[:, :, :], is_k[:, 0]).then_inc(s["r_taken"], 1)
            for k in range(1, TOPK):
                eng.wait_ge(s["r_taken"], k)
                eng.tensor_tensor(taken[:, :, :], taken[:, :, :], is_k[:, k], ALU.add).then_inc(s["r_taken"], 1)
            eng.wait_ge(s["r_exp"], 1)
            step(eng.tensor_reduce(top_sum[:, :], top[:, :, :], axis=AX.X, op=ALU.add))
            step(eng.reciprocal(top_sum[:, :], top_sum[:, :]))
            step(eng.tensor_tensor(weight[:, :, :], top[:, :, :], top_sum[:, :].unsqueeze(2).to_broadcast([P, NB, TOPK]),
                                   ALU.mult))
            eng.wait_ge(s["r_counted"], 1)
            step(eng.tensor_copy(total[:, :, :].rearrange("p e b -> p b e"), p_total[:, :, :]))
            step(eng.tensor_tensor_scan(upto[:, :, :].rearrange("p e b -> p (e b)"),
                                        same_e[:, :, :].rearrange("p e b -> p (e b)"),
                                        total[:, :, :].rearrange("p e b -> p (e b)"), 0.0, ALU.mult, ALU.add))
            step(eng.tensor_tensor(rank[:, :, :], upto[:, :, :], total[:, :, :], ALU.subtract))
            step(eng.tensor_tensor(rank[:, :, :], rank[:, :, :], p_rank[:, :, :].rearrange("p b e -> p e b"), ALU.add))
            step(eng.tensor_scalar(region[:, :], expert_i[:, :], float(REGION), None, ALU.mult))

            def places(start, dst, ready):
                step(eng.tensor_tensor(base[:, :, :], rank[:, :, :], start.unsqueeze(2).to_broadcast([P, E, NB]), ALU.add))
                for k in range(TOPK):
                    step(eng.tensor_tensor(hit[:, :, :], is_k[:, k], base[:, :, :].rearrange("p e b -> p b e"), ALU.mult))
                    step(eng.tensor_reduce(place_f[:, k, :], hit[:, :, :], axis=AX.X, op=ALU.add))
                    eng.tensor_copy(dst[:, :, k], place_f[:, k, :]).then_inc(s[ready], 1)

            places(region[:, :], place_in, "in_ready")
            count = upto[:, :, NB - 1:NB]
            step(eng.tensor_tensor(over[:, :, :], count.to_broadcast([P, E, TOK // UT]),
                                   size_i[:, :].unsqueeze(1).to_broadcast([P, E, TOK // UT]), ALU.is_gt))
            step(eng.tensor_reduce(n_units[:, :], over[:, :, :], axis=AX.X, op=ALU.add))
            step(eng.tensor_tensor_scan(unit_end[:, :], ones[:, 0:E], n_units[:, :], 0.0, ALU.mult, ALU.add))
            step(eng.tensor_tensor(start_row[:, :], unit_end[:, :], n_units[:, :], ALU.subtract))
            step(eng.tensor_scalar(start_row[:, :], start_row[:, :], float(UT), None, ALU.mult))
            places(start_row[:, :], place, "place_ready")
            step(eng.tensor_scalar(last_unit[:, :], unit_end[:, E - 1:E], 1.0, None, ALU.subtract))
            step(eng.tensor_scalar(unit_f[:, 0, :], unit_i[:, :], last_unit[:, 0:1], None, ALU.min))
            step(eng.tensor_tensor(past[:, :, :], unit_f[:, 0, :].unsqueeze(2).to_broadcast([P, NU, E]),
                                   unit_end[:, :].unsqueeze(1).to_broadcast([P, NU, E]), ALU.is_ge))
            step(eng.tensor_reduce(unit_f[:, 1, :], past[:, :, :], axis=AX.X, op=ALU.add))
            step(eng.tensor_scalar(skip[:, :], n_units[:, :], float(-UT), float(REGION), ALU.mult, ALU.add))
            step(eng.tensor_tensor(past_skip[:, :, :], past[:, :, :],
                                   skip[:, :].unsqueeze(1).to_broadcast([P, NU, E]), ALU.mult))
            step(eng.tensor_reduce(unit_f[:, 2, :], past_skip[:, :, :], axis=AX.X, op=ALU.add))
            step(eng.scalar_tensor_tensor(out=unit_f[:, 2, :], in0=unit_f[:, 0, :], scalar=float(UT),
                                          in1=unit_f[:, 2, :], op0=ALU.mult, op1=ALU.add))
            eng.tensor_copy(units[:, 0, :], unit_f[:, 1, :]).then_inc(s["unit_ready"], 1)
            eng.tensor_copy(units[:, 1, :], unit_f[:, 2, :]).then_inc(s["unit_ready"], 1)
            step(eng.tensor_tensor(tail_f[:, :], region[:, :], upto[:, :, NB - 1], ALU.add))
            eng.tensor_copy(tail[:, :], tail_f[:, :]).then_inc(s["unit_ready"], 1)


def experts(nc, outer, t, xs_d, ys_d, ident, units, w_gu, w_dn):
    with ExitStack() as ctx:
        def sb(name, shape, dt=F32):
            return ctx.enter_context(nc.sbuf_tensor(name, shape, dt))

        b_gu = sb("b_gu", [P, E, 2 * KF])
        b_dn = sb("b_dn", [P, E, DM])
        x_rows = sb("x_rows", [P, 2, UB, DM])
        x_hi = [sb(f"x_hi{i}", [P, KD, UT], F32R) for i in range(2)]
        x_lo = sb("x_lo", [P, KD, UT], F32R)
        gu_hi = [sb(f"gu_hi{i}", [P, KD, 2 * FF], F32R) for i in range(2)]
        gu_lo = [sb(f"gu_lo{i}", [P, KD, 2 * FF], F32R) for i in range(2)]
        dn_hi = sb("dn_hi", [P, KF, DM], F32R)
        dn_lo = sb("dn_lo", [P, KF, DM], F32R)
        gate = sb("gate", [P, KF, UT])
        up = sb("up", [P, 2, UT])
        act_hi = [sb(f"act_hi{i}", [P, KF, UT], F32R) for i in range(2)]
        act_lo = [sb(f"act_lo{i}", [P, KF, UT], F32R) for i in range(2)]
        res = sb("res", [P, UB, DM])

        p_x = ctx.enter_context(nc.psum_tensor("p_x", [P, KD, UT], F32))
        p_g = ctx.enter_context(nc.psum_tensor("p_g", [P, 2, UT], F32))
        p_u = ctx.enter_context(nc.psum_tensor("p_u", [P, 2, UT], F32))
        p_o = ctx.enter_context(nc.psum_tensor("p_o", [P, 2, UT], F32))

        names = """e_loaded e_carrier xr_loaded xrT_done xhi_done xlo_done guhi_done gulo_done dnhi_done dnlo_done
            gate_mm up_mm gu_used gate_lim up_out silu_done up_lim act_done acthi_done actlo_done
            down_mm res_done ys_stored""".split()
        s = {n: outer.enter_context(nc.semaphore(n)) for n in names}
        block = ctx.enter_context(nc.Block())

        def steps(eng, body):
            def run_of(lo):
                return {"prep": lo < NU, "mid": 1 <= lo < NU + 1, "down": 2 <= lo}
            first = 3
            pairs = (NU - 1 - first) // 2
            for v in range(first):
                body(Span(v, v, v), v % 2, run_of(v))
            with eng.Fori(0, pairs) as i:
                for v in (first, first + 1):
                    body(Span(i * 2 + v, v, 2 * (pairs - 1) + v), v % 2, run_of(v))
            for v in range(first + 2 * pairs, NU + 2):
                body(Span(v, v, v), v % 2, run_of(v))

        def expert_of(eng, j):
            return eng.value_load(units[0:1, 0, bass.ds(j.i, 1)], min_val=0, max_val=E - 1)

        @block.sync
        def _(eng):
            def hold(sem, at, f):
                wait(eng, sem, at, f)
                alone(eng, s["e_carrier"])

            def row_of(j):
                return eng.value_load(units[0:1, 1, bass.ds(j.i, 1)], min_val=0, max_val=E * REGION - UT)

            def load(j, par):
                hold(s["xr_loaded"], j, lambda i: 16 * i)
                hold(s["xrT_done"], j, lambda i: i - 1)
                eng.dma_start(x_rows[:, par], xs_d[bass.ds(row_of(j), UT), :].rearrange("(t p) d -> p t d", p=P))\
                   .then_inc(s["xr_loaded"], 16)

            def store(j):
                hold(s["ys_stored"], j, lambda i: 16 * i)
                hold(s["res_done"], j, lambda i: UB * (i + 1))
                eng.dma_start(ys_d[bass.ds(j.i * UT, UT), :].rearrange("(t p) d -> p t d", p=P), res[:, :, :])\
                   .then_inc(s["ys_stored"], 16)

            eng.dma_start(b_gu[:, :, :], t["b_gu"]).then_inc(s["e_loaded"], 16)
            eng.dma_start(b_dn[:, :, :], t["b_dn"].partition_broadcast(P)).then_inc(s["e_loaded"], 16)
            load(Span(0, 0, 0), 0)

            def body(at, par, run):
                if run["prep"] and at.hi < NU - 1:
                    load(at + 1, 1 - par)
                if run["down"]:
                    store(at + -2)

            steps(eng, body)
            eng.wait_ge(s["ys_stored"], 16 * NU)

        @block.tensor
        def _(eng):
            def turn(j, par):
                wait(eng, s["xr_loaded"], j, lambda i: 16 * (i + 1))
                wait(eng, s["xhi_done"], j, lambda i: i)
                wait(eng, s["xlo_done"], j, lambda i: i)
                for k in range(KD):
                    for tb in range(UB):
                        mm = eng.transpose(p_x[:, k, tb * P:(tb + 1) * P], x_rows[:, par, tb, k * P:(k + 1) * P], ident[:, :])
                mm.then_inc(s["xrT_done"], 1)

            def split_product(dst, pairs):
                terms = [v for ah, al, bh, bl in pairs for v in ((ah, bh), (ah, bl), (al, bh))]
                for n, (a, b) in enumerate(terms):
                    mm = eng.matmul(dst, a, b, start=(n == 0), stop=(n == len(terms) - 1))
                return mm

            def gate_up(j, m, buf):
                if m == 0:
                    wait(eng, s["xlo_done"], j, lambda i: i + 1)
                    wait(eng, s["gulo_done"], j, lambda i: KD * (i + 1))
                    wait(eng, s["guhi_done"], j, lambda i: i + 1)
                wait(eng, s["gate_lim"], j, lambda i: KF * i + m - 1)
                for psum, off, done in ((p_g, 0, "gate_mm"), (p_u, FF, "up_mm")):
                    if psum is p_u:
                        wait(eng, s["up_out"], j, lambda i: KF * i + m - 1)
                    cols = slice(off + m * P, off + (m + 1) * P)
                    split_product(psum[:, m % 2, :],
                                  [(gu_hi[buf][:, k, cols], gu_lo[buf][:, k, cols], x_hi[buf][:, k, :], x_lo[:, k, :])
                                   for k in range(KD)]).then_inc(s[done], 1)

            def down(j, tb, buf):
                if tb == 0:
                    wait(eng, s["actlo_done"], j, lambda i: KF * (i + 1))
                    wait(eng, s["dnlo_done"], j, lambda i: i + 1)
                wait(eng, s["res_done"], j, lambda i: UB * i + tb - 1)
                cols = slice(tb * P, (tb + 1) * P)
                split_product(p_o[:, tb % 2, 0:DM],
                              [(act_hi[buf][:, m, cols], act_lo[buf][:, m, cols], dn_hi[:, m, :], dn_lo[:, m, :])
                               for m in range(KF)]).then_inc(s["down_mm"], 1)

            eng.wait_ge(s["e_loaded"], 32)

            def body(at, par, run):
                for m in range(KF):
                    if run["mid"]:
                        gate_up(at + -1, m, 1 - par)
                    if run["prep"] and m == 0:
                        turn(at, par)
                if run["down"]:
                    for tb in range(UB):
                        down(at + -2, tb, par)

            steps(eng, body)

        @block.scalar
        def _(eng):
            def x_high(j, buf):
                wait(eng, s["xrT_done"], j, lambda i: i + 1)
                wait(eng, s["up_mm"], j, lambda i: KF * (i - 1))
                wait(eng, s["xlo_done"], j, lambda i: i - 1)
                eng.activation(x_hi[buf][:, :, :], p_x[:, :, :], ACT.Copy).then_inc(s["xhi_done"], 1)

            def gu_high(j, buf, e):
                wait(eng, s["up_mm"], j, lambda i: KF * (i - 1))
                wait(eng, s["gulo_done"], j, lambda i: KD * (i - 1))
                eng.activation(gu_hi[buf][:, :, :], w_gu[:, bass.ds(e, 1)].rearrange("p a k f -> p (a k) f"),
                               ACT.Copy).then_inc(s["guhi_done"], 1)

            def dn_high(j, e):
                wait(eng, s["down_mm"], j, lambda i: UB * i)
                wait(eng, s["dnlo_done"], j, lambda i: i)
                eng.activation(dn_hi[:, :, :], w_dn[:, bass.ds(e, 1)].rearrange("p a k d -> p (a k) d"),
                               ACT.Copy).then_inc(s["dnhi_done"], 1)

            def up_copy(j, m, e):
                wait(eng, s["up_mm"], j, lambda i: KF * i + m + 1)
                wait(eng, s["act_done"], j, lambda i: KF * i + m - 1)
                eng.activation(up[:, m % 2, :], p_u[:, m % 2, :], ACT.Identity,
                               bias=b_gu[:, bass.ds(e, 1), KF + m:KF + m + 1].rearrange("p a b -> p (a b)"))\
                   .then_inc(s["up_out"], 1)

            def silu(j, m):
                wait(eng, s["gate_lim"], j, lambda i: KF * i + m + 1)
                eng.activation(gate[:, m, :], gate[:, m, :], ACT.Silu, scale=ALPHA).then_inc(s["silu_done"], 1)

            def act_high(j, m, buf):
                wait(eng, s["act_done"], j, lambda i: KF * i + m + 1)
                wait(eng, s["down_mm"], j, lambda i: UB * (i - 1))
                wait(eng, s["actlo_done"], j, lambda i: KF * (i - 1) + m + 1)
                eng.activation(act_hi[buf][:, m, :], gate[:, m, :], ACT.Copy).then_inc(s["acthi_done"], 1)

            eng.wait_ge(s["e_loaded"], 32)

            def body(at, par, run):
                mid, down = at + -1, at + -2
                if run["prep"]:
                    e_prep = expert_of(eng, at)
                if run["mid"]:
                    e_mid = expert_of(eng, mid)
                if run["down"]:
                    dn_high(down, expert_of(eng, down))
                if run["mid"]:
                    up_copy(mid, 0, e_mid)
                    silu(mid, 0)
                if run["prep"]:
                    gu_high(at, par, e_prep)
                if run["mid"]:
                    for m in range(1, KF):
                        up_copy(mid, m, e_mid)
                        silu(mid, m)
                        act_high(mid, m - 1, 1 - par)
                        if m == 1 and run["prep"]:
                            x_high(at, par)
                    act_high(mid, KF - 1, 1 - par)
                elif run["prep"]:
                    x_high(at, par)

            steps(eng, body)

        @block.vector
        def _(eng):
            def gate_limit(j, m, e):
                wait(eng, s["gate_mm"], j, lambda i: KF * i + m + 1)
                wait(eng, s["actlo_done"], j, lambda i: KF * (i - 1) + m + 1)
                eng.tensor_scalar(gate[:, m, :], p_g[:, m % 2, :],
                                  b_gu[:, bass.ds(e, 1), m:m + 1].rearrange("p a b -> p (a b)"), LIMIT,
                                  ALU.add, ALU.min).then_inc(s["gate_lim"], 1)

            def up_limit(j, m):
                wait(eng, s["up_out"], j, lambda i: KF * i + m + 1)
                eng.tensor_scalar(up[:, m % 2, :], up[:, m % 2, :], LIMIT, -LIMIT, ALU.min, ALU.max)\
                   .then_inc(s["up_lim"], 1)

            def act_of(j, m):
                wait(eng, s["up_lim"], j, lambda i: KF * i + m + 1)
                wait(eng, s["silu_done"], j, lambda i: KF * i + m + 1)
                eng.scalar_tensor_tensor(out=gate[:, m, :], in0=up[:, m % 2, :], scalar=1.0, in1=gate[:, m, :],
                                         op0=ALU.add, op1=ALU.mult).then_inc(s["act_done"], 1)

            def x_low(j, buf):
                wait(eng, s["xhi_done"], j, lambda i: i + 1)
                wait(eng, s["up_mm"], j, lambda i: KF * i)
                eng.tensor_tensor(x_lo[:, :, :], p_x[:, :, :], x_hi[buf][:, :, :].bitcast(F32), ALU.subtract).then_inc(s["xlo_done"], 1)

            def result(j, tb, e):
                wait(eng, s["down_mm"], j, lambda i: UB * i + tb + 1)
                if tb == 0:
                    wait(eng, s["ys_stored"], j, lambda i: 16 * i)
                eng.scalar_tensor_tensor(out=res[:, tb, :], in0=p_o[:, tb % 2, 0:DM], scalar=1.0 / ALPHA,
                                         in1=b_dn[:, bass.ds(e, 1), :].rearrange("p a d -> p (a d)"),
                                         op0=ALU.mult, op1=ALU.add).then_inc(s["res_done"], 1)

            eng.wait_ge(s["e_loaded"], 32)

            def body(at, par, run):
                mid, down = at + -1, at + -2
                if run["mid"]:
                    e_mid = expert_of(eng, mid)
                    for m in range(KF + 1):
                        if m < KF:
                            gate_limit(mid, m, e_mid)
                        if m:
                            up_limit(mid, m - 1)
                            act_of(mid, m - 1)
                if run["down"]:
                    e_down = expert_of(eng, down)
                    result(down, 0, e_down)
                    result(down, 1, e_down)
                if run["prep"]:
                    x_low(at, par)
                if run["down"]:
                    result(down, 2, e_down)
                    result(down, 3, e_down)

            steps(eng, body)

        @block.gpsimd
        def _(eng):
            def gu_low(j, k, buf, e):
                wait(eng, s["guhi_done"], j, lambda i: i + 1)
                eng.tensor_tensor(gu_lo[buf][:, k, :], w_gu[:, bass.ds(e, 1), k, :].rearrange("p a f -> p (a f)"),
                                  gu_hi[buf][:, k, :].bitcast(F32), ALU.subtract).then_inc(s["gulo_done"], 1)

            def dn_low(j, e):
                wait(eng, s["dnhi_done"], j, lambda i: i + 1)
                eng.tensor_tensor(dn_lo[:, :, :], w_dn[:, bass.ds(e, 1)].rearrange("p a k d -> p (a k) d"),
                                  dn_hi[:, :, :].bitcast(F32), ALU.subtract).then_inc(s["dnlo_done"], 1)

            def act_low(j, m, buf):
                wait(eng, s["acthi_done"], j, lambda i: KF * i + m + 1)
                eng.tensor_tensor(act_lo[buf][:, m, :], gate[:, m, :], act_hi[buf][:, m, :].bitcast(F32),
                                  ALU.subtract).then_inc(s["actlo_done"], 1)

            def body(at, par, run):
                mid, down = at + -1, at + -2
                if run["prep"]:
                    e_prep = expert_of(eng, at)
                if run["down"]:
                    dn_low(down, expert_of(eng, down))
                if run["mid"]:
                    act_low(mid, 0, 1 - par)
                if run["prep"]:
                    gu_low(at, 0, par, e_prep)
                if run["mid"]:
                    act_low(mid, 1, 1 - par)
                if run["prep"]:
                    gu_low(at, 1, par, e_prep)
                if run["mid"]:
                    act_low(mid, 2, 1 - par)
                    act_low(mid, 3, 1 - par)

            steps(eng, body)


def combine(nc, outer, x1_d, ys_d, place, weight, out):
    with ExitStack() as ctx:
        def sb(name, shape, dt=F32):
            return ctx.enter_context(nc.sbuf_tensor(name, shape, dt))

        rows = sb("rows4", [P, 2, TOPK, DM])
        x1 = sb("x1_again", [P, 2, DM])
        mix = sb("mix", [P, 2, DM])
        final = sb("final", [P, 2, DM])
        st = sb("st", [P, 6])
        agg = sb("agg", [P, 2])
        mv = sb("mv", [P, 2, 4])
        c_eps = sb("c_eps", [P, 1])
        place_now = sb("place_now2", [P, 2, TOPK], I32)

        names = "got0 got1 got2 got3 c_const c_carrier c_carrier_pool c_carrier_sp c_now x1_loaded mixed c_stats c_aggr c_mv c_ln c_rstd c_norm c_done out_stored".split()
        s = {n: outer.enter_context(nc.semaphore(n)) for n in names}
        got = [s[f"got{k}"] for k in range(TOPK)]
        block = ctx.enter_context(nc.Block())

        def two(buf, b):
            return buf[:, bass.ds(b.i % 2, 1), :].rearrange("p a d -> p (a d)")

        def col(b, c, n=1):
            return mv[:, bass.ds(b.i % 2, 1), c:c + n].rearrange("p a c -> p (a c)")

        def blocks(eng, body):
            body(Span(0, 0, 0), True, False)
            for v in (1, 2):
                body(Span(v, v, v), True, True)
            with eng.Fori(3, NB) as i:
                body(Span(i, 3, NB - 1), True, True)
            body(Span(NB, NB, NB), False, True)

        @block.sync
        def _(eng):
            def hold(sem, at, f):
                wait(eng, sem, at, f)
                alone(eng, s["c_carrier_sp"])

            def body(at, begin, end):
                if begin:
                    hold(s["x1_loaded"], at, lambda i: 16 * i)
                    hold(s["c_done"], at, lambda i: i - 1)
                    eng.dma_start(two(x1, at), x1_d[bass.ds(at.i * P, P), :]).then_inc(s["x1_loaded"], 16)
                if end:
                    b = at + -1
                    hold(s["out_stored"], b, lambda i: 16 * i)
                    hold(s["c_done"], b, lambda i: i + 1)
                    eng.dma_start(out[bass.ds(b.i * P, P), :], two(final, b)).then_inc(s["out_stored"], 16)

            blocks(eng, body)
            eng.wait_ge(s["out_stored"], 16 * NB)

        @block.gpsimd
        def _(eng):
            def fetch(b, half):
                wait(eng, s["c_now"], b, lambda i: i + 1)
                for k in range(TOPK):
                    wait(eng, got[k], b, lambda i: 16 * i)
                    wait(eng, s["mixed"], b, lambda i: TOPK * (i - 2) + k + 1)
                    alone(eng, s["c_carrier_pool"])
                    eng.indirect_dma_start(
                        out=rows[:, half, k, :], out_offset=None,
                        in_=ys_d, in_offset=bass.IndirectOffsetOnAxis(ap=place_now[:, half, k:k + 1], axis=0),
                    ).then_inc(got[k], 16)

            for half in range(2):
                fetch(Span(half, half, half), half)
            with eng.Fori(1, NB // 2) as i:
                for half in range(2):
                    fetch(Span(i * 2 + half, 2 + half, NB - 2 + half), half)

        @block.scalar
        def _(eng):
            eng.preload_act_table_set("natural_log_exp_and_others")
            eng.wait_ge(s["c_const"], 1)

            def rstd(b):
                wait(eng, s["c_mv"], b, lambda i: i + 1)
                eng.activation(col(b, 2), col(b, 1), ACT.Ln, bias=c_eps[:, 0:1]).then_inc(s["c_ln"], 1)
                wait(eng, s["c_ln"], b, lambda i: i + 1)
                eng.activation(col(b, 3), col(b, 2), ACT.Exp, scale=-0.5).then_inc(s["c_rstd"], 1)

            def places(b, half):
                for k in range(TOPK):
                    wait(eng, got[k], b, lambda i: 16 * (i - 1))
                eng.activation(place_now[:, half, :], place[:, bass.ds(b.i, 1), :].rearrange("p a k -> p (a k)"),
                               ACT.Copy).then_inc(s["c_now"], 1)

            for half in range(2):
                places(Span(half, half, half), half)
            with eng.Fori(0, NB // 2 - 1) as i:
                for half in range(2):
                    b = Span(i * 2 + half, half, NB - 4 + half)
                    places(b + 2, half)
                    rstd(b)
            for v in (NB - 2, NB - 1):
                rstd(Span(v, v, v))

        @block.vector
        def _(eng):
            eng.memset(c_eps[:, :], EPS).then_inc(s["c_const"], 1)

            def begin_block(b):
                w = weight[:, bass.ds(b.i, 1), :].rearrange("p a k -> p (a k)")
                for k in range(TOPK):
                    wait(eng, got[k], b, lambda i: 16 * (i + 1))
                    row = rows[:, bass.ds(b.i % 2, 1), k, :].rearrange("p a d -> p (a d)")
                    if k == 0:
                        eng.tensor_scalar(two(mix, b), row, w[:, 0:1], None, ALU.mult).then_inc(s["mixed"], 1)
                    else:
                        wait(eng, s["mixed"], b, lambda i: TOPK * i + k)
                        eng.scalar_tensor_tensor(out=two(mix, b), in0=row, scalar=w[:, k:k + 1], in1=two(mix, b),
                                                 op0=ALU.mult, op1=ALU.add).then_inc(s["mixed"], 1)
                wait(eng, s["mixed"], b, lambda i: TOPK * (i + 1))
                alone(eng, s["c_carrier"])
                eng.bn_stats(st[:, :], two(mix, b)).then_inc(s["c_stats"], 1)
                wait(eng, s["c_stats"], b, lambda i: i + 1)
                alone(eng, s["c_carrier"])
                eng.bn_aggr(agg[:, :], st[:, :]).then_inc(s["c_aggr"], 1)
                wait(eng, s["c_aggr"], b, lambda i: i + 1)
                eng.tensor_copy(col(b, 0, 2), agg[:, :]).then_inc(s["c_mv"], 1)

            def end_block(b):
                wait(eng, s["c_rstd"], b, lambda i: i + 1)
                eng.tensor_scalar(two(mix, b), two(mix, b), col(b, 0), col(b, 3), ALU.subtract, ALU.mult).then_inc(s["c_norm"], 1)
                wait(eng, s["c_norm"], b, lambda i: i + 1)
                wait(eng, s["x1_loaded"], b, lambda i: 16 * (i + 1))
                wait(eng, s["out_stored"], b, lambda i: 16 * (i - 1))
                eng.tensor_tensor(two(final, b), two(mix, b), two(x1, b), ALU.add).then_inc(s["c_done"], 1)

            def body(at, begin, end):
                if begin:
                    wait(eng, s["c_done"], at, lambda i: i - 1)
                    begin_block(at)
                if end:
                    end_block(at + -1)

            blocks(eng, body)



DEBUG = False


def kernel(**inputs):
    import numpy as _np
    import concourse.bacc as _bacc
    from concourse import mybir as _mybir
    from concourse.bass_utils import run_bass_kernel_spmd as _run

    a = {k[3:] if k.startswith("L0_") else k: _np.asarray(v) for k, v in inputs.items()}

    def tiles(w):
        return w.reshape(-1, 128, w.shape[-1]).transpose(1, 0, 2)

    def column(v):
        return v.reshape(-1, 128).T

    chan = [column(a["attn_conv_b"]), column(a["attn_D"]), column(a["attn_b_dt"])]
    chan += [column(a["attn_conv_w"][:, 0, k]) for k in range(TAPS)]
    laid = {
        "x": a["attn_x"].reshape(TOK, DM),
        "w_in": tiles(a["attn_W_in"]), "w_x": tiles(a["attn_W_xproj"]), "w_dt": a["attn_W_dt"],
        "w_out": tiles(a["attn_W_out"]), "w_r": tiles(a["ffn_router_weight"].T),
        "ln_gb": _np.stack([column(a["attn_ln_g"]), column(a["attn_ln_b"])], 1),
        "chan": _np.stack(chan, 1), "a_log": tiles(a["attn_A_log"]), "rbias": a["ffn_router_bias"],
        "w_gu": a["ffn_gate_up_proj"].transpose(0, 2, 1), "b_gu": a["ffn_gate_up_proj_bias"].reshape(E, 2 * KF, P).transpose(2, 0, 1),
        "w_dn": a["ffn_down_proj"].transpose(0, 2, 1), "b_dn": a["ffn_down_proj_bias"],
    }
    nc = _bacc.Bacc("TRN2", target_bir_lowering=False, num_devices=1,
                    dynamic_dma_scratch_size=4096)
    arrays, t = {}, {}
    for name, v in laid.items():
        v = _np.ascontiguousarray(v)
        arrays["in_" + name] = v
        t[name] = nc.dram_tensor("in_" + name, v.shape, _mybir.dt.from_np(v.dtype), kind="ExternalInput").ap()
    out = nc.dram_tensor("out_0", (TOK, DM), F32, kind="ExternalOutput").ap()
    sandwich(nc, t, out, DEBUG)
    r = _run(nc, [arrays], core_ids=[0])
    return r.results[0]["out_0"].reshape(BATCH, L, DM)
```
